# Optimizing a Trainium2 kernel written in Bass

```python
import numpy as np
import jax
import jax.numpy as jnp

def _softmax(x, axis=-1):
    return jax.nn.softmax(x, axis=axis)

def _gelu(x):
    return jax.nn.gelu(x, approximate=True)

def _silu(x):
    return jax.nn.silu(x)

def _sigmoid(x):
    return jax.nn.sigmoid(x)

def _layernorm(x, axis=-1, eps=1e-05):
    m = jnp.mean(x, axis=axis, keepdims=True)
    v = jnp.var(x, axis=axis, keepdims=True)
    return (x - m) / jnp.sqrt(v + eps)

def _scatter_add(tgt, idx, src, axis=0):
    return tgt.at[idx].add(src)

def _segment_sum(src, seg, n):
    return jax.ops.segment_sum(src, seg, n)
kernel_name = 'mk_dlrm_tower_d1_rec_r8_80108f'

def setup_inputs(seed: int=0):
    np.random.seed(seed)
    _w = jnp.asarray

    def _rec_inputs():
        import jax
        import jax.numpy as jnp
        _tk = jax.random.key(seed)
        ids = jnp.stack([jax.random.randint(jax.random.fold_in(_tk, 200 + f), (2048,), 0, v, jnp.int32) for f, v in enumerate([1250, 125000, 1000, 1000, 12500, 1000, 12500, 1000, 1250, 1000, 1250, 1250, 1250, 1000, 1250, 1250, 1250, 1000, 1000, 1000, 12500, 1000, 1000, 1250, 1250, 12500])], axis=1)
        tbl_0 = 0.05 * jax.random.normal(jax.random.fold_in(_tk, 500 + 0), (1250, 128), jnp.float32)
        tbl_1 = 0.05 * jax.random.normal(jax.random.fold_in(_tk, 500 + 1), (125000, 128), jnp.float32)
        tbl_2 = 0.05 * jax.random.normal(jax.random.fold_in(_tk, 500 + 2), (1000, 128), jnp.float32)
        tbl_3 = 0.05 * jax.random.normal(jax.random.fold_in(_tk, 500 + 3), (1000, 128), jnp.float32)
        tbl_4 = 0.05 * jax.random.normal(jax.random.fold_in(_tk, 500 + 4), (12500, 128), jnp.float32)
        tbl_5 = 0.05 * jax.random.normal(jax.random.fold_in(_tk, 500 + 5), (1000, 128), jnp.float32)
        tbl_6 = 0.05 * jax.random.normal(jax.random.fold_in(_tk, 500 + 6), (12500, 128), jnp.float32)
        tbl_7 = 0.05 * jax.random.normal(jax.random.fold_in(_tk, 500 + 7), (1000, 128), jnp.float32)
        tbl_8 = 0.05 * jax.random.normal(jax.random.fold_in(_tk, 500 + 8), (1250, 128), jnp.float32)
        tbl_9 = 0.05 * jax.random.normal(jax.random.fold_in(_tk, 500 + 9), (1000, 128), jnp.float32)
        tbl_10 = 0.05 * jax.random.normal(jax.random.fold_in(_tk, 500 + 10), (1250, 128), jnp.float32)
        tbl_11 = 0.05 * jax.random.normal(jax.random.fold_in(_tk, 500 + 11), (1250, 128), jnp.float32)
        tbl_12 = 0.05 * jax.random.normal(jax.random.fold_in(_tk, 500 + 12), (1250, 128), jnp.float32)
        tbl_13 = 0.05 * jax.random.normal(jax.random.fold_in(_tk, 500 + 13), (1000, 128), jnp.float32)
        tbl_14 = 0.05 * jax.random.normal(jax.random.fold_in(_tk, 500 + 14), (1250, 128), jnp.float32)
        tbl_15 = 0.05 * jax.random.normal(jax.random.fold_in(_tk, 500 + 15), (1250, 128), jnp.float32)
        tbl_16 = 0.05 * jax.random.normal(jax.random.fold_in(_tk, 500 + 16), (1250, 128), jnp.float32)
        tbl_17 = 0.05 * jax.random.normal(jax.random.fold_in(_tk, 500 + 17), (1000, 128), jnp.float32)
        tbl_18 = 0.05 * jax.random.normal(jax.random.fold_in(_tk, 500 + 18), (1000, 128), jnp.float32)
        tbl_19 = 0.05 * jax.random.normal(jax.random.fold_in(_tk, 500 + 19), (1000, 128), jnp.float32)
        tbl_20 = 0.05 * jax.random.normal(jax.random.fold_in(_tk, 500 + 20), (12500, 128), jnp.float32)
        tbl_21 = 0.05 * jax.random.normal(jax.random.fold_in(_tk, 500 + 21), (1000, 128), jnp.float32)
        tbl_22 = 0.05 * jax.random.normal(jax.random.fold_in(_tk, 500 + 22), (1000, 128), jnp.float32)
        tbl_23 = 0.05 * jax.random.normal(jax.random.fold_in(_tk, 500 + 23), (1250, 128), jnp.float32)
        tbl_24 = 0.05 * jax.random.normal(jax.random.fold_in(_tk, 500 + 24), (1250, 128), jnp.float32)
        tbl_25 = 0.05 * jax.random.normal(jax.random.fold_in(_tk, 500 + 25), (12500, 128), jnp.float32)
        _rk = jax.random.fold_in(_tk, 7)
        r_dense_features = -0.000520686 + 1.00062 * jax.random.normal(jax.random.fold_in(_rk, 101), (2048, 128), jnp.float32)
        W_top1 = 0.0405887 * jax.random.normal(jax.random.fold_in(_tk, 801), (607, 512), jnp.float32)
        W_top2 = 0.0441942 * jax.random.normal(jax.random.fold_in(_tk, 802), (512, 256), jnp.float32)
        W_top3 = 0.0625 * jax.random.normal(jax.random.fold_in(_tk, 803), (256, 1), jnp.float32)
        b_top1 = jnp.zeros((512,), jnp.float32)
        b_top2 = jnp.zeros((256,), jnp.float32)
        return (r_dense_features, ids, tbl_0, tbl_1, tbl_2, tbl_3, tbl_4, tbl_5, tbl_6, tbl_7, tbl_8, tbl_9, tbl_10, tbl_11, tbl_12, tbl_13, tbl_14, tbl_15, tbl_16, tbl_17, tbl_18, tbl_19, tbl_20, tbl_21, tbl_22, tbl_23, tbl_24, tbl_25, W_top1, b_top1, W_top2, b_top2, W_top3)
    r_dense_features, ids, tbl_0, tbl_1, tbl_2, tbl_3, tbl_4, tbl_5, tbl_6, tbl_7, tbl_8, tbl_9, tbl_10, tbl_11, tbl_12, tbl_13, tbl_14, tbl_15, tbl_16, tbl_17, tbl_18, tbl_19, tbl_20, tbl_21, tbl_22, tbl_23, tbl_24, tbl_25, W_top1, b_top1, W_top2, b_top2, W_top3 = _rec_inputs()

    def _L0_rec_setup():
        import jax, jax.numpy as jnp
        import numpy as np
        B, F, D = (2048, 26, 128)
        key = jax.random.key(seed)
        k1, k2 = jax.random.split(key)
        dense_features = jax.random.normal(k1, (B, D), dtype=jnp.float32)
        sparse_values = jax.random.normal(k2, (B, F, D), dtype=jnp.float32)
        return {'dense_features': dense_features, 'sparse_values': sparse_values}
    _L0_rec_all = _L0_rec_setup()
    _L0_rec_in = {k: v for k, v in _L0_rec_all.items() if k in ()}
    del _L0_rec_all
    return {'r_dense_features': r_dense_features, 'ids': ids, 'tbl_0': tbl_0, 'tbl_1': tbl_1, 'tbl_2': tbl_2, 'tbl_3': tbl_3, 'tbl_4': tbl_4, 'tbl_5': tbl_5, 'tbl_6': tbl_6, 'tbl_7': tbl_7, 'tbl_8': tbl_8, 'tbl_9': tbl_9, 'tbl_10': tbl_10, 'tbl_11': tbl_11, 'tbl_12': tbl_12, 'tbl_13': tbl_13, 'tbl_14': tbl_14, 'tbl_15': tbl_15, 'tbl_16': tbl_16, 'tbl_17': tbl_17, 'tbl_18': tbl_18, 'tbl_19': tbl_19, 'tbl_20': tbl_20, 'tbl_21': tbl_21, 'tbl_22': tbl_22, 'tbl_23': tbl_23, 'tbl_24': tbl_24, 'tbl_25': tbl_25, 'W_top1': W_top1, 'b_top1': b_top1, 'W_top2': W_top2, 'b_top2': b_top2, 'W_top3': W_top3}

def reference(r_dense_features, ids, tbl_0, tbl_1, tbl_2, tbl_3, tbl_4, tbl_5, tbl_6, tbl_7, tbl_8, tbl_9, tbl_10, tbl_11, tbl_12, tbl_13, tbl_14, tbl_15, tbl_16, tbl_17, tbl_18, tbl_19, tbl_20, tbl_21, tbl_22, tbl_23, tbl_24, tbl_25, W_top1, b_top1, W_top2, b_top2, W_top3):
    import jax
    import jax.numpy as jnp

    def _L0_rec_ref(dense_features, sparse_values):
        import jax, jax.numpy as jnp
        import numpy as np
        B, F, D = (2048, 26, 128)
        sd = jnp.einsum('bfd,bd->bf', sparse_values, dense_features)
        ss = jnp.einsum('bfd,bgd->bfg', sparse_values, sparse_values)
        iu, ju = jnp.triu_indices(F, k=1)
        pairs = ss[:, iu, ju]
        return jnp.concatenate([dense_features, sd, pairs], axis=1)
    e = jnp.stack([tbl_0[ids[:, 0]], tbl_1[ids[:, 1]], tbl_2[ids[:, 2]], tbl_3[ids[:, 3]], tbl_4[ids[:, 4]], tbl_5[ids[:, 5]], tbl_6[ids[:, 6]], tbl_7[ids[:, 7]], tbl_8[ids[:, 8]], tbl_9[ids[:, 9]], tbl_10[ids[:, 10]], tbl_11[ids[:, 11]], tbl_12[ids[:, 12]], tbl_13[ids[:, 13]], tbl_14[ids[:, 14]], tbl_15[ids[:, 15]], tbl_16[ids[:, 16]], tbl_17[ids[:, 17]], tbl_18[ids[:, 18]], tbl_19[ids[:, 19]], tbl_20[ids[:, 20]], tbl_21[ids[:, 21]], tbl_22[ids[:, 22]], tbl_23[ids[:, 23]], tbl_24[ids[:, 24]], tbl_25[ids[:, 25]]], axis=1)
    z = _L0_rec_ref(r_dense_features, e)
    z = z.reshape(z.shape[0], -1)
    h = jnp.concatenate([z, r_dense_features], axis=1)
    h = jnp.maximum(h @ W_top1 + b_top1, 0.0)
    h = jnp.maximum(h @ W_top2 + b_top2, 0.0)
    y = h @ W_top3
    return y

_drawn_inputs = setup_inputs


def setup_inputs(seed=0):
    import zlib

    import numpy as np

    out = dict(_drawn_inputs(seed))
    spreads = {'b_top1': (0.0, 0.1), 'b_top2': (0.0, 0.1)}
    factors = {}
    for name, (base, spread) in spreads.items():
        noise = np.random.default_rng([zlib.crc32(name.encode()), seed]).standard_normal(out[name].shape)
        drawn = base * np.exp(spread * noise) if base else spread * noise
        out[name] = jnp.asarray(drawn.astype(out[name].dtype))
    for name, factor in factors.items():
        out[name] = (out[name] * factor).astype(out[name].dtype)
    return out
```

```python
from contextlib import ExitStack

import concourse.bass as bass
from concourse import mybir

P = 128
Q = 32
F32 = mybir.dt.float32
I32 = mybir.dt.int32
ACT = mybir.ActivationFunctionType
ALU = mybir.AluOpType


def dlrm_tower(nc, dense, ids, tables, w_top1, b_top1, w_top2, b_top2, w_top3, out):
    B, D = dense.shape
    F = len(tables)
    NF = F + 1
    H1, H2 = w_top1.shape[1], w_top2.shape[1]
    U = 4
    BLOCKS = B // (U * P)
    BS = U * P
    NG = 4
    NCOL = 28
    CH = NCOL // 4
    TG = 4
    TGROUPS = -(-NF // TG)
    UG = 8
    UNITS = P // (NG * UG)
    N1, N2 = H1 // P, H2 // P
    assert D == P and F < NCOL <= Q and B == BLOCKS * BS

    with ExitStack() as ctx:
        def sb(name, shape, dt=F32):
            return ctx.enter_context(nc.sbuf_tensor(name, shape, dt))

        def psum(name, shape):
            return ctx.enter_context(nc.psum_tensor(name, shape, F32))

        def sem(name):
            return ctx.enter_context(nc.semaphore(name))

        ident = sb("ident", [P, P])
        ids_sb = sb("ids_sb", [P, U, F], I32)
        rows = sb("rows", [P, U, NF, D])
        xt = sb("xt", [P, 2, P, Q])
        dense_t = sb("dense_t", [P, BS])
        feat = sb("feat", [P, CH, BS])
        w1_pairs = sb("w1_pairs", [P, CH, H1])
        w1_dense = sb("w1_dense", [P, 2, H1])
        w1_x = sb("w1_x", [P, H1])
        w2 = sb("w2", [P, N1, H2])
        w3 = sb("w3", [P, N2])
        b1 = sb("b1", [P, N1])
        b2 = sb("b2", [P, N2])
        h1 = sb("h1", [P, N1, BS])
        h2 = sb("h2", [P, N2, BS])
        y = sb("y", [1, B])

        ps_t = [psum(f"ps_t{i}", [P, TG * P]) for i in range(2)]
        ps_g = [psum(f"ps_g{i}", [P, UG, P]) for i in range(2)]
        ps_m = [psum(f"ps_m{i}", [P, BS]) for i in range(2)]

        ident_zero, ident_ready = sem("ident_zero"), sem("ident_ready")
        pads_ready = sem("pads_ready")
        w1_zero, w1_loaded, w1_summed = sem("w1_zero"), sem("w1_loaded"), sem("w1_summed")
        wx_loaded, wr_loaded = sem("wx_loaded"), sem("wr_loaded")
        ids_loaded = [sem(f"ids_loaded{u}") for u in range(U)]
        dense_loaded = [sem(f"dense_loaded{u}") for u in range(U)]
        gathered = [sem(f"gathered{u}") for u in range(U)]
        tiles_begun = sem("tiles_begun")
        slot_free = sem("slot_free")
        t_ready = [sem(f"t_ready{i}") for i in range(2)]
        t_free = [sem(f"t_free{i}") for i in range(2)]
        g_ready = sem("g_ready")
        g_free = [sem(f"g_free{i}") for i in range(2)]
        m_ready = [sem(f"m_ready{i}") for i in range(2)]
        m_free = [sem(f"m_free{i}") for i in range(2)]
        y_stored = sem("y_stored")

        block = ctx.enter_context(nc.Block())

        def pair_row(a, b):
            return D + F + a * (F - 1) - a * (a - 1) // 2 + b - a - 1

        @block.gpsimd
        def _(pool):
            pool.wait_ge(ident_zero, 1)
            nc.gpsimd.affine_select(out=ident[:, :], in_=ident[:, :], compare_op=ALU.not_equal, fill=1.0,
                                    base=0, pattern=[[-1, P]], channel_multiplier=1).then_inc(ident_ready, 1)
            with pool.Fori(0, BLOCKS) as s:
                for u in range(U):
                    pool.wait_ge(ids_loaded[u], 16 * (s + 1))
                    pool.wait_ge(slot_free, U * s + u + 1)
                    pool.sem_inc(tiles_begun, 1)
                    for f in range(F):
                        pool.indirect_dma_start(
                            rows[:, u, f, :], None, tables[f],
                            bass.IndirectOffsetOnAxis(ids_sb[:, u, f:f + 1], 0)).then_inc(gathered[u], 16)

        @block.sync
        def _(sp):
            with sp.Fori(0, BLOCKS) as s:
                for u in range(U):
                    sp.wait_ge(slot_free, U * s + u + 1)
                    sp.dma_start(ids_sb[:, u, :], ids[bass.ds(s * BS + u * P, P), :]).then_inc(ids_loaded[u], 16)
                    sp.dma_start(rows[:, u, F, :], dense[bass.ds(s * BS + u * P, P), :])\
                        .then_inc(dense_loaded[u], 16)
            sp.wait_ge(y_stored, 16 * BLOCKS)

        def move_transposed(eng, copy, parity, s, u):
            for k in range(TGROUPS):
                m = TGROUPS * u + k
                if m % 2 != parity:
                    continue
                n = min(TG, NF - TG * k)
                eng.wait_ge(t_ready[parity], TGROUPS * U // 2 * s + m // 2 + 1)
                src = ps_t[parity][:, 0:n * P].rearrange("p (f b) -> p b f", f=n)
                if k == TGROUPS - 1:
                    copy(dense_t[:, u * P:(u + 1) * P], ps_t[parity][:, (n - 1) * P:n * P])
                copy(xt[:, u % 2, :, TG * k:TG * k + n], src).then_inc(t_free[parity], 1)

        def move_gram(eng, copy, mine, quads, s, u):
            for v in range(UNITS):
                eng.wait_ge(g_ready, UNITS * (U * s + u) + v + 1)
                for q in quads:
                    for j in range(4):
                        src = ps_g[v % 2][Q * q:Q * q + Q, :, q * NCOL:(q + 1) * NCOL]\
                            .rearrange("p i (c j) -> p j i c", j=4)[:, j]
                        b = u * P + v * NG * UG + q
                        dst = feat[Q * j:Q * j + Q, :, b:b + NG * (UG - 1) + 1:NG].rearrange("p c i -> p i c")
                        last = copy(dst, src)
                last.then_inc(g_free[mine], 1)

        @block.vector
        def _(dve):
            nc.vector.memset(ident[:, :], 0.0).then_inc(ident_zero, 1)
            dve.sem_inc(slot_free, U)
            dve.sem_inc(t_free[0], 1)
            dve.sem_inc(g_free[0], 2)
            dve.sem_inc(m_free[1], 1)
            nc.vector.memset(xt[:, :, :, NF:Q], 0.0).then_inc(pads_ready, 1)
            nc.vector.memset(w1_pairs[:, :, :], 0.0).then_inc(w1_zero, 1)
            dve.wait_ge(wx_loaded, 32)
            nc.vector.tensor_tensor(w1_x[:, :], w1_dense[:, 0, :], w1_dense[:, 1, :], ALU.add)\
                .then_inc(w1_summed, 1)
            dve.wait_ge(wr_loaded, 16 * (N1 + N2 + N2 + 1))
            with dve.Fori(0, BLOCKS) as s:
                for u in range(U):
                    move_transposed(dve, nc.vector.tensor_copy, 0, s, u)
                    move_gram(dve, nc.vector.tensor_copy, 0, (0, 1), s, u)
                for k, (dst, bias) in enumerate([(h1[:, 1], b1[:, 1:2]), (h1[:, 3], b1[:, 3:4]),
                                                 (h2[:, 1], b2[:, 1:2])]):
                    dve.wait_ge(m_ready[1], 3 * s + k + 1)
                    nc.vector.tensor_scalar(dst, ps_m[1][:, :], bias, 0.0, ALU.add, ALU.max)\
                        .then_inc(m_free[1], 1)

        @block.scalar
        def _(act):
            act.sem_inc(t_free[1], 1)
            act.sem_inc(g_free[1], 2)
            act.sem_inc(m_free[0], 1)
            act.dma_start(w1_dense[:, 0, :], w_top1[0:D, :]).then_inc(wx_loaded, 16)
            act.dma_start(w1_dense[:, 1, :], w_top1[w_top1.shape[0] - D:, :]).then_inc(wx_loaded, 16)
            act.wait_ge(w1_zero, 1)
            for a in range(F - 1):
                c, j = a // 4, a % 4
                act.dma_start(w1_pairs[Q * j + a + 1:Q * j + F, c, :],
                              w_top1[pair_row(a, a + 1):pair_row(a, F - 1) + 1, :]).then_inc(w1_loaded, 16)
            for j in range(4):
                n = len(range(j, F, 4))
                act.dma_start(w1_pairs[Q * j + F:Q * j + F + 1, 0:n, :],
                              w_top1[D + j:D + F:4, :].unsqueeze(0)).then_inc(w1_loaded, 16)
            act.dma_start(w2[:, :, :], w_top2.rearrange("(k p) n -> p k n", p=P)).then_inc(wr_loaded, 16)
            for k in range(N2):
                act.dma_start(w3[:, k:k + 1], w_top3[k * P:(k + 1) * P, :]).then_inc(wr_loaded, 16)
            for k in range(N1):
                act.dma_start(b1[:, k:k + 1], b_top1[k * P:(k + 1) * P].unsqueeze(1)).then_inc(wr_loaded, 16)
            for k in range(N2):
                act.dma_start(b2[:, k:k + 1], b_top2[k * P:(k + 1) * P].unsqueeze(1)).then_inc(wr_loaded, 16)
            act.wait_ge(wr_loaded, 16 * (N1 + N2 + N2 + 1))
            with act.Fori(0, BLOCKS) as s:
                for u in range(U):
                    move_transposed(act, nc.scalar.copy, 1, s, u)
                    move_gram(act, nc.scalar.copy, 1, (2, 3), s, u)
                for k, (dst, bias) in enumerate([(h1[:, 0], b1[:, 0:1]), (h1[:, 2], b1[:, 2:3]),
                                                 (h2[:, 0], b2[:, 0:1])]):
                    act.wait_ge(m_ready[0], 4 * s + k + 1)
                    nc.scalar.activation(dst, ps_m[0][:, :], ACT.Relu, bias=bias).then_inc(m_free[0], 1)
                act.wait_ge(m_ready[0], 4 * s + 4)
                nc.scalar.copy(y[:, bass.ds(s * BS, BS)], ps_m[0][0:1, :]).then_inc(m_free[0], 1)
                act.wait_ge(m_free[0], 4 * s + 5)
                act.dma_start(out[bass.ds(s * BS, BS), :].rearrange("b o -> o b"),
                              y[:, bass.ds(s * BS, BS)]).then_inc(y_stored, 16)

        @block.tensor
        def _(pe):
            pe.wait_ge(ident_ready, 1)
            pe.wait_ge(pads_ready, 1)
            with pe.Fori(0, BLOCKS) as s:
                for u in range(U):
                    pe.wait_ge(dense_loaded[u], 16 * (s + 1))
                    pe.wait_ge(gathered[u], 16 * F * (s + 1))
                    for k in range(TGROUPS):
                        m = TGROUPS * u + k
                        pe.wait_ge(t_free[m % 2], TGROUPS * U // 2 * s + m // 2 + 1)
                        for i in range(min(TG, NF - TG * k)):
                            last = nc.tensor.transpose(ps_t[m % 2][:, i * P:(i + 1) * P],
                                                       rows[:, u, TG * k + i, :], ident[:, :])
                        last.then_inc(t_ready[m % 2], 1)
                    for i in range(2):
                        pe.wait_ge(t_free[i], TGROUPS * U // 2 * s + (TGROUPS * (u + 1) + 1 - i) // 2 + 1)
                    for v in range(UNITS):
                        for i in range(2):
                            pe.wait_ge(g_free[i], UNITS * U * s + UNITS * u + v + 1)
                        for i in range(UG):
                            b = (v * UG + i) * NG
                            last = nc.tensor.matmul(
                                ps_g[v % 2][:, i, 0:NG * NCOL],
                                xt[:, u % 2, b:b + NG, :],
                                xt[:, u % 2, b:b + NG, 0:NCOL], start=True, stop=True)
                            if v == 0 and i == 0:
                                last.then_inc(slot_free, 1)
                        last.then_inc(g_ready, 1)
                pe.wait_ge(w1_summed, 1)
                pe.wait_ge(w1_loaded, 16 * (F - 1 + 4))
                pe.wait_ge(wr_loaded, 16 * (N1 + N2 + N2 + 1))
                for i in range(2):
                    pe.wait_ge(g_free[i], UNITS * U * (s + 1) + 2)
                for n in range(N1):
                    per = 4 if n % 2 == 0 else 3
                    pe.wait_ge(m_free[n % 2], per * s + n // 2 + 1)
                    nc.tensor.matmul(ps_m[n % 2][:, :], w1_x[:, n * P:(n + 1) * P], dense_t[:, :],
                                     start=True, stop=False)
                    for c in range(CH):
                        last = nc.tensor.matmul(ps_m[n % 2][:, :], w1_pairs[:, c, n * P:(n + 1) * P],
                                                feat[:, c, :], start=False, stop=(c == CH - 1))
                    last.then_inc(m_ready[n % 2], 1)
                for i in range(2):
                    pe.wait_ge(m_free[i], (4 - i) * s + 3)
                for n in range(N2):
                    for k in range(N1):
                        last = nc.tensor.matmul(ps_m[n][:, :], w2[:, k, n * P:(n + 1) * P], h1[:, k, :],
                                                start=(k == 0), stop=(k == N1 - 1))
                    last.then_inc(m_ready[n], 1)
                for i in range(2):
                    pe.wait_ge(m_free[i], (4 - i) * s + 4)
                for k in range(N2):
                    last = nc.tensor.matmul(ps_m[0][0:1, :], w3[:, k:k + 1], h2[:, k, :],
                                            start=(k == 0), stop=(k == N2 - 1))
                last.then_inc(m_ready[0], 1)


_TABLES = 26
_INS = (["r_dense_features", "ids"] + [f"tbl_{f}" for f in range(_TABLES)]
        + ["W_top1", "b_top1", "W_top2", "b_top2", "W_top3"])


def kernel(**inputs):
    import numpy as np
    import concourse.bacc as bacc
    from concourse.bass_utils import run_bass_kernel_spmd

    nc = bacc.Bacc("TRN2", target_bir_lowering=False, num_devices=1)
    arrays, ap = {}, {}
    for name in _INS:
        a = np.ascontiguousarray(inputs[name])
        arrays[f"in_{name}"] = a
        ap[name] = nc.dram_tensor(f"in_{name}", a.shape, mybir.dt.from_np(a.dtype), kind="ExternalInput").ap()
    out = nc.dram_tensor("out_y", (inputs["ids"].shape[0], 1), F32, kind="ExternalOutput").ap()
    dlrm_tower(nc, ap["r_dense_features"], ap["ids"], [ap[f"tbl_{f}"] for f in range(_TABLES)],
               ap["W_top1"], ap["b_top1"], ap["W_top2"], ap["b_top2"], ap["W_top3"], out)
    r = run_bass_kernel_spmd(nc, [arrays], core_ids=[0])
    return r.results[0]["out_y"]
```

```python
from contextlib import ExitStack

import concourse.bass as bass
from concourse import mybir

P = 128
Q = 32
F32 = mybir.dt.float32
F32R = mybir.dt.float32r
I32 = mybir.dt.int32
ACT = mybir.ActivationFunctionType
ALU = mybir.AluOpType

PICKED = (2, 3, 17, 18)


def runs(fields):
    out = []
    for at, f in enumerate(fields):
        if out and out[-1][1] + out[-1][2] == f:
            out[-1][2] += 1
        else:
            out.append([at, f, 1])
    return out


def part(n, places, i):
    return range(n * i // places, n * (i + 1) // places)


def dlrm_tower(nc, dense, ids, ids_t, tables, w_top1, b_top1, w_top2, b_top2, w_top3, out):
    B, D = dense.shape
    F = len(tables)
    NF = F + 1
    H1, H2 = w_top1.shape[1], w_top2.shape[1]
    U = 4
    BS = U * P
    BLOCKS = B // BS
    NG = 4
    NCOL = 28
    CH = NCOL // 4
    UG = 8
    UNITS = P // (NG * UG)
    N1, N2 = H1 // P, H2 // P
    turned = [f for f in range(NF) if f not in PICKED]
    TG = 4
    TGROUPS = -(-len(turned) // TG)
    NT = TGROUPS * U // 2
    NP = len(PICKED)
    V = tables[PICKED[0]].shape[0]
    VC = 8
    VP = V // VC
    RING = 4
    LOOKS = NP * VC
    TILE_LOOKS = 3
    TILE_PLACES = 2 + UNITS
    LAYER_LOOKS = LOOKS - U * TILE_LOOKS
    L1_PLACES = 3
    LAYER_PLACES = 1 + N1 * L1_PLACES + 1 + N1 + 1
    assert all(tables[f].shape[0] == V for f in PICKED) and V == VC * VP and VP <= P and VC % RING == 0
    assert D == P and F < NCOL <= Q and B == BLOCKS * BS and TGROUPS * U % 2 == 0 and BLOCKS > 1

    with ExitStack() as ctx:
        def sb(name, shape, dt=F32):
            return ctx.enter_context(nc.sbuf_tensor(name, shape, dt))

        def psum(name, shape):
            return ctx.enter_context(nc.psum_tensor(name, shape, F32))

        def sem(name):
            return ctx.enter_context(nc.semaphore(name))

        ident = sb("ident", [P, P])
        ids_sb = sb("ids_sb", [P, B // P, F], I32)
        ids_now = sb("ids_now", [P, U, F], I32)
        rows = sb("rows", [P, U, len(turned), D])
        xt = sb("xt", [P, P, Q])
        looked = sb("looked", [P, 2, NP, BS])
        raw = sb("raw", [VP, 2, VC, D])
        tbl_hi = sb("tbl_hi", [VP, 2, VC, D], F32R)
        tbl_lo = sb("tbl_lo", [VP, 2, VC, D], F32R)
        ids_row = sb("ids_row", [P, 2, BS], I32)
        onehot = sb("onehot", [VP, RING, BS], F32R)
        row_no = sb("row_no", [P, VC])
        feat = sb("feat", [P, CH, P])
        feat_hi = sb("feat_hi", [P, CH, BS], F32R)
        feat_lo = sb("feat_lo", [P, CH, BS], F32R)
        x_hi = sb("x_hi", [P, BS], F32R)
        x_lo = sb("x_lo", [P, BS], F32R)
        w1_hi = sb("w1_hi", [P, CH, H1], F32R)
        w1_lo = sb("w1_lo", [P, CH, H1], F32R)
        w1x_hi = sb("w1x_hi", [P, H1], F32R)
        w1x_lo = sb("w1x_lo", [P, H1], F32R)
        w2 = sb("w2", [P, N1, H2])
        w3 = sb("w3", [P, N2])
        b1 = sb("b1", [P, N1])
        b2 = sb("b2", [P, N2])
        h1 = sb("h1", [P, N1, BS])
        h2 = sb("h2", [P, N2, BS])
        y = sb("y", [1, BS])

        late = U - 2
        assert 2 * len(turned) * D >= (CH + 2) * H1
        w1_raw = rows[:, late:U].rearrange("p u f d -> p (u f d)")[:, 0:(CH + 2) * H1]\
            .rearrange("p (c n) -> p c n", n=H1)

        ps_t = [psum(f"ps_t{i}", [P, TG * P]) for i in range(2)]
        ps_g = [psum(f"ps_g{i}", [P, UG, P]) for i in range(2)]
        ps_m, ps_l = psum("ps_m", [P, BS]), psum("ps_l", [P, BS])

        ident_zero, ident_ready = sem("ident_zero"), sem("ident_ready")
        row_no_ready = sem("row_no_ready")
        pads_ready = sem("pads_ready")
        w1_zero, w1_loaded, wx_loaded = sem("w1_zero"), sem("w1_loaded"), sem("wx_loaded")
        wx_summed, w1_hi_ready, w1_lo_ready = sem("wx_summed"), sem("w1_hi_ready"), sem("w1_lo_ready")
        wr_loaded = sem("wr_loaded")
        ids_loaded, ids_copied = sem("ids_loaded"), sem("ids_copied")
        tiles_begun = sem("tiles_begun")
        dense_loaded = [sem(f"dense_loaded{u}") for u in range(U)]
        gathered = [sem(f"gathered{u}") for u in range(U)]
        slot_free = sem("slot_free")
        raw_loaded = [sem(f"raw_loaded{i}") for i in range(2)]
        hi_ready, lo_ready = sem("hi_ready"), sem("lo_ready")
        onehot_ready = sem("onehot_ready")
        onehot_begun = sem("onehot_begun")
        l_ready, l_free = sem("l_ready"), sem("l_free")
        m_ready, m_free = sem("m_ready"), sem("m_free")
        filled = sem("filled")
        t_ready = [sem(f"t_ready{i}") for i in range(2)]
        t_free = [sem(f"t_free{i}") for i in range(2)]
        g_ready = sem("g_ready")
        g_free = [sem(f"g_free{i}") for i in range(2)]
        f_hi_ready, f_lo_ready = sem("f_hi_ready"), sem("f_lo_ready")
        y_stored = sem("y_stored")

        block = ctx.enter_context(nc.Block())

        def pair_row(a, b):
            return D + F + a * (F - 1) - a * (a - 1) // 2 + b - a - 1

        def before(k):
            return 2 if k >= 2 else k + NP - max(x for x in range(NP) if x % 2 == k % 2)

        def turns_done(i, s, u):
            return NT * s + len(range(i, TGROUPS * (u + 1), 2)) + 1

        def tile_looks(u, i):
            return [u * TILE_LOOKS + x for x in part(TILE_LOOKS, TILE_PLACES, i)]

        def layer_looks(i):
            return [U * TILE_LOOKS + x for x in part(LAYER_LOOKS, LAYER_PLACES, i)]

        @block.gpsimd
        def _(pool):
            pool.wait_ge(ident_zero, 1)
            nc.gpsimd.affine_select(out=ident[:, :], in_=ident[:, :], compare_op=ALU.not_equal, fill=1.0,
                                    base=0, pattern=[[-1, P]], channel_multiplier=1).then_inc(ident_ready, 1)
            nc.gpsimd.iota(row_no[:, :], pattern=[[1, VC]], base=0, channel_multiplier=VC,
                           allow_small_or_imprecise_dtypes=True).then_inc(row_no_ready, 1)
            pool.wait_ge(ids_loaded, 16)
            with pool.Fori(0, BLOCKS) as s:
                for u in range(U):
                    pool.wait_ge(slot_free, U * s + u + 1)
                    nc.gpsimd.tensor_copy(ids_now[:, u, :], ids_sb[:, U * s + u, :]).then_inc(ids_copied, 1)
                    pool.wait_ge(ids_copied, U * s + u + 1)
                    pool.sem_inc(tiles_begun, 1)
                    for at, f in enumerate(turned[:-1]):
                        pool.indirect_dma_start(
                            rows[:, u, at, :], None, tables[f],
                            bass.IndirectOffsetOnAxis(ids_now[:, u, f:f + 1], 0)).then_inc(gathered[u], 16)

        @block.sync
        def _(sp):
            def load_lookup(blk, k, first=False):
                b, f = k % 2, PICKED[k]
                if not (first and k < 2):
                    sp.wait_ge(onehot_ready, VC * (NP * blk + k - before(k) + 1))
                src = tables[f].rearrange("(p c) d -> p c d", c=VC)
                most = VP // 16 * 16
                sp.dma_start(raw[0:most, b], src[0:most]).then_inc(raw_loaded[b], 16)
                sp.dma_start(raw[most:VP, b], src[most:VP]).then_inc(raw_loaded[b], 16)
                sp.dma_start(ids_row[:, b, :], ids_t[f:f + 1, bass.ds(blk * BS, BS)].broadcast_to([P, BS]))\
                    .then_inc(raw_loaded[b], 16)

            sp.dma_start(ids_sb[:, :, :], ids.rearrange("(t p) f -> p t f", p=P)).then_inc(ids_loaded, 16)
            for k in range(NP):
                load_lookup(0, k, first=True)
            with sp.Fori(0, BLOCKS - 1) as s:
                for k in range(NP):
                    load_lookup(s + 1, k)
            sp.wait_ge(y_stored, 16 * (BLOCKS + 1))

        def move_transposed(eng, copy, parity, s, u, groups):
            for k in groups:
                m = TGROUPS * u + k
                if m % 2 != parity:
                    continue
                group = turned[TG * k:TG * k + TG]
                eng.wait_ge(t_ready[parity], NT * s + m // 2 + 1)
                for at, f, n in runs(group):
                    last = copy(xt[:, :, f:f + n],
                                ps_t[parity][:, at * P:(at + n) * P].rearrange("p (f b) -> p b f", f=n))
                last.then_inc(t_free[parity], 1)

        def move_gram(eng, copy, mine, quads, s, u, v):
            eng.wait_ge(g_ready, UNITS * (U * s + u) + v + 1)
            for q in quads:
                for j in range(4):
                    src = ps_g[v % 2][Q * q:Q * q + Q, :, q * NCOL:(q + 1) * NCOL]\
                        .rearrange("p i (c j) -> p j i c", j=4)[:, j]
                    b = v * NG * UG + q
                    dst = feat[Q * j:Q * j + Q, :, b:b + NG * (UG - 1) + 1:NG].rearrange("p c i -> p i c")
                    last = copy(dst, src)
            last.then_inc(g_free[mine], 1)

        @block.vector
        def _(dve):
            def move_looked(blk, k):
                dve.wait_ge(l_ready, NP * blk + k + 1)
                nc.vector.tensor_copy(looked[:, blk % 2, k, :], ps_l[:, :]).then_inc(l_free, 1)

            def make_onehots(blk, chunks):
                for x in chunks:
                    k, c = divmod(x, VC)
                    b = k % 2
                    if c == 0:
                        dve.wait_ge(hi_ready, NP * blk + k + 1)
                        nc.vector.tensor_tensor(tbl_lo[:, b], raw[:, b], tbl_hi[:, b].bitcast(F32),
                                                ALU.subtract).then_inc(lo_ready, 1)
                    dve.wait_ge(onehot_begun, LOOKS * blk + x + 1)
                    nc.vector.tensor_tensor(onehot[:, c % RING, :], ids_row[0:VP, b, :],
                                            row_no[0:VP, c:c + 1].broadcast_to([VP, BS]),
                                            ALU.is_equal).then_inc(onehot_ready, 1)
                    if c == 0 and k > 0:
                        move_looked(blk, k - 1)

            def block_steps(s, look):
                def split_feat(u):
                    dve.wait_ge(f_hi_ready, U * s + u + 1)
                    nc.vector.tensor_tensor(feat_lo[:, :, u * P:(u + 1) * P], feat[:, :, :],
                                            feat_hi[:, :, u * P:(u + 1) * P].bitcast(F32),
                                            ALU.subtract).then_inc(f_lo_ready, 1)

                for u in range(U):
                    move_transposed(dve, nc.vector.tensor_copy, 0, s, u, range(2))
                    if look:
                        make_onehots(s + 1, tile_looks(u, 0))
                    move_transposed(dve, nc.vector.tensor_copy, 0, s, u, range(2, 4))
                    if look:
                        make_onehots(s + 1, tile_looks(u, 1))
                    move_transposed(dve, nc.vector.tensor_copy, 0, s, u, range(4, TGROUPS))
                    if u > 0:
                        split_feat(u - 1)
                    dve.wait_ge(t_free[1], turns_done(1, s, u))
                    bs = slice(u * P, (u + 1) * P)
                    nc.vector.tensor_tensor(x_lo[:, bs], xt[:, :, F], x_hi[:, bs].bitcast(F32), ALU.subtract)
                    for v in range(UNITS):
                        if look:
                            make_onehots(s + 1, tile_looks(u, 2 + v))
                        if u > 0 and v == 0:
                            dve.wait_ge(f_lo_ready, U * s + u)
                        move_gram(dve, nc.vector.tensor_copy, 0, (0, 1), s, u, v)
                if look:
                    make_onehots(s + 1, layer_looks(0))
                split_feat(U - 1)
                if look:
                    for i in range(1, LAYER_PLACES):
                        make_onehots(s + 1, layer_looks(i))
                    move_looked(s + 1, NP - 1)
                else:
                    for k, (dst, bias) in enumerate([(h1[:, 1], b1[:, 1:2]), (h1[:, 3], b1[:, 3:4]),
                                                     (h2[:, 1], b2[:, 1:2])]):
                        dve.wait_ge(l_ready, NP * BLOCKS + k + 1)
                        nc.vector.tensor_scalar(dst, ps_l[:, :], bias, 0.0, ALU.add, ALU.max)\
                            .then_inc(l_free, 1)

            nc.vector.memset(ident[:, :], 0.0).then_inc(ident_zero, 1)
            dve.sem_inc(slot_free, late)
            dve.sem_inc(t_free[0], 1)
            dve.sem_inc(g_free[0], 2)
            dve.sem_inc(l_free, 1)
            dve.sem_inc(onehot_begun, RING - 1)
            nc.vector.memset(w1_raw[:, 0:CH, :], 0.0).then_inc(w1_zero, 1)
            nc.vector.memset(xt[:, :, NF:Q], 0.0).then_inc(pads_ready, 1)
            dve.wait_ge(row_no_ready, 1)
            make_onehots(0, range(LOOKS // 2))
            dve.wait_ge(wx_loaded, 32)
            nc.vector.tensor_tensor(w1_raw[:, CH, :], w1_raw[:, CH, :], w1_raw[:, CH + 1, :], ALU.add)\
                .then_inc(wx_summed, 1)
            dve.wait_ge(w1_hi_ready, 2)
            nc.vector.tensor_tensor(w1_lo[:, :, :], w1_raw[:, 0:CH, :], w1_hi[:, :, :].bitcast(F32),
                                    ALU.subtract).then_inc(w1_lo_ready, 1)
            nc.vector.tensor_tensor(w1x_lo[:, :], w1_raw[:, CH, :], w1x_hi[:, :].bitcast(F32), ALU.subtract)\
                .then_inc(w1_lo_ready, 1)
            dve.wait_ge(w1_lo_ready, 2)
            dve.sem_inc(slot_free, U - late)
            make_onehots(0, range(LOOKS // 2, LOOKS))
            move_looked(0, NP - 1)
            dve.wait_ge(wr_loaded, 16 * (N1 + N2 + N2 + 1))
            with dve.Fori(0, BLOCKS - 1) as s:
                block_steps(s, True)
            block_steps(BLOCKS - 1, False)

        @block.scalar
        def _(act):
            def split_table(blk, k, first=False):
                b = k % 2
                act.wait_ge(raw_loaded[b], 48 * (len(range(b, NP, 2)) * blk + k // 2 + 1))
                if not (first and k < 2):
                    act.wait_ge(l_ready, NP * blk + k - before(k) + 1)
                nc.scalar.copy(tbl_hi[:, b], raw[:, b]).then_inc(hi_ready, 1)

            def split_tables(blk, chunks, first=False):
                for x in chunks:
                    if x % VC == VC // 2 and x // VC + 1 < NP:
                        split_table(blk, x // VC + 1, first)

            def load_dense(s, u):
                act.dma_start(rows[:, u, len(turned) - 1, :], dense[bass.ds(s * BS + u * P, P), :])\
                    .then_inc(dense_loaded[u], 16)

            def block_steps(s, look):
                def split_feat(u):
                    for i in range(2):
                        act.wait_ge(g_free[i], UNITS * (U * s + u + 1) + 2)
                    nc.scalar.copy(feat_hi[:, :, u * P:(u + 1) * P], feat[:, :, :]).then_inc(f_hi_ready, 1)

                if look:
                    split_table(s + 1, 0)
                for u in range(U):
                    bs = slice(u * P, (u + 1) * P)
                    for i in range(2):
                        if look:
                            split_tables(s + 1, tile_looks(u, i))
                    move_transposed(act, nc.scalar.copy, 1, s, u, range(2))
                    if u > 0:
                        split_feat(u - 1)
                    move_transposed(act, nc.scalar.copy, 1, s, u, range(2, TGROUPS - 2))
                    act.wait_ge(l_free, NP * (s + 1) + 1)
                    for at, f, n in runs(PICKED):
                        last = nc.scalar.copy(xt[:, :, f:f + n],
                                              looked[:, s % 2, at:at + n, bs].rearrange("p f b -> p b f"))
                    last.then_inc(filled, 1)
                    m = TGROUPS * (u + 1) - 1
                    at = len(turned) - 1 - TG * (TGROUPS - 1)
                    act.wait_ge(t_ready[m % 2], NT * s + m // 2 + 1)
                    nc.scalar.copy(x_hi[:, bs], ps_t[m % 2][:, at * P:(at + 1) * P])
                    move_transposed(act, nc.scalar.copy, 1, s, u, range(TGROUPS - 2, TGROUPS))
                    for v in range(UNITS):
                        if look:
                            split_tables(s + 1, tile_looks(u, 2 + v))
                        if v == 0:
                            if u > 0:
                                act.wait_ge(f_lo_ready, U * s + u)
                        move_gram(act, nc.scalar.copy, 1, (2, 3), s, u, v)
                    if look:
                        load_dense(s + 1, u)
                split_feat(U - 1)
                outs = [(h1[:, n], b1[:, n:n + 1]) for n in range(N1)] + [(h2[:, n], b2[:, n:n + 1])
                                                                        for n in range(N2)]
                done = (N1 + N2 + 1) * s
                place = 0
                if look:
                    split_tables(s + 1, layer_looks(0))
                    place = 1
                for k, (dst, bias) in enumerate(outs):
                    if not look and k % 2:
                        continue
                    if look:
                        n = L1_PLACES if k < N1 else N1 // N2
                        if k == N1:
                            n += 1
                        for i in range(n):
                            split_tables(s + 1, layer_looks(place + i))
                        place += n
                    done = done + 1
                    act.wait_ge(m_ready, done)
                    nc.scalar.activation(dst, ps_m[:, :], ACT.Relu, bias=bias).then_inc(m_free, 1)
                if look:
                    split_tables(s + 1, layer_looks(place))
                    assert place + 1 == LAYER_PLACES
                act.wait_ge(m_ready, done + 1)
                act.wait_ge(y_stored, 16 * (s + 1))
                nc.scalar.copy(y[:, :], ps_m[0:1, :]).then_inc(m_free, 1)
                act.wait_ge(m_free, done + 2)
                act.dma_start(out[bass.ds(s * BS, BS), :].rearrange("b o -> o b"), y[:, :]).then_inc(y_stored, 16)

            act.sem_inc(t_free[1], 1)
            act.sem_inc(g_free[1], 2)
            act.sem_inc(m_free, 1)
            act.sem_inc(y_stored, 16)
            for u in range(late):
                load_dense(0, u)
            split_table(0, 0, first=True)
            act.dma_start(w1_raw[:, CH, :], w_top1[0:D, :]).then_inc(wx_loaded, 16)
            act.dma_start(w1_raw[:, CH + 1, :], w_top1[w_top1.shape[0] - D:, :]).then_inc(wx_loaded, 16)
            act.wait_ge(w1_zero, 1)
            for a in range(F - 1):
                c, j = a // 4, a % 4
                act.dma_start(w1_raw[Q * j + a + 1:Q * j + F, c, :],
                              w_top1[pair_row(a, a + 1):pair_row(a, F - 1) + 1, :]).then_inc(w1_loaded, 16)
            for j in range(4):
                n = len(range(j, F, 4))
                act.dma_start(w1_raw[Q * j + F:Q * j + F + 1, 0:n, :],
                              w_top1[D + j:D + F:4, :].unsqueeze(0)).then_inc(w1_loaded, 16)
            act.dma_start(w2[:, :, :], w_top2.rearrange("(k p) n -> p k n", p=P)).then_inc(wr_loaded, 16)
            for k in range(N2):
                act.dma_start(w3[:, k:k + 1], w_top3[k * P:(k + 1) * P, :]).then_inc(wr_loaded, 16)
            for k in range(N1):
                act.dma_start(b1[:, k:k + 1], b_top1[k * P:(k + 1) * P].unsqueeze(1)).then_inc(wr_loaded, 16)
            for k in range(N2):
                act.dma_start(b2[:, k:k + 1], b_top2[k * P:(k + 1) * P].unsqueeze(1)).then_inc(wr_loaded, 16)
            split_tables(0, range(LOOKS // 2), first=True)
            act.wait_ge(w1_loaded, 16 * (F - 1 + 4))
            nc.scalar.copy(w1_hi[:, :, :], w1_raw[:, 0:CH, :]).then_inc(w1_hi_ready, 1)
            act.wait_ge(wx_summed, 1)
            nc.scalar.copy(w1x_hi[:, :], w1_raw[:, CH, :]).then_inc(w1_hi_ready, 1)
            split_tables(0, range(LOOKS // 2, LOOKS), first=True)
            act.wait_ge(w1_lo_ready, 2)
            for u in range(late, U):
                load_dense(0, u)
            act.wait_ge(wr_loaded, 16 * (N1 + N2 + N2 + 1))
            with act.Fori(0, BLOCKS - 1) as s:
                block_steps(s, True)
            block_steps(BLOCKS - 1, False)

        @block.tensor
        def _(pe):
            def look_up(blk, chunks):
                for x in chunks:
                    k, c = divmod(x, VC)
                    b = k % 2
                    if c == 0:
                        pe.wait_ge(l_free, NP * blk + k + 1)
                        pe.wait_ge(lo_ready, NP * blk + k + 1)
                    pe.wait_ge(onehot_ready, LOOKS * blk + x + 1)
                    nc.tensor.matmul(ps_l[:, :], tbl_hi[:, b, c, :], onehot[:, c % RING, :],
                                     start=(c == 0), stop=False).then_inc(onehot_begun, 1)
                    last = nc.tensor.matmul(ps_l[:, :], tbl_lo[:, b, c, :], onehot[:, c % RING, :],
                                            start=False, stop=(c == VC - 1))
                    if c == VC - 1:
                        last.then_inc(l_ready, 1)

            def block_steps(s, look):
                for u in range(U):
                    pe.wait_ge(dense_loaded[u], 16 * (s + 1))
                    pe.wait_ge(gathered[u], 16 * (len(turned) - 1) * (s + 1))
                    for k in range(TGROUPS):
                        m = TGROUPS * u + k
                        pe.wait_ge(t_free[m % 2], NT * s + m // 2 + 1)
                        for i in range(min(TG, len(turned) - TG * k)):
                            last = nc.tensor.transpose(ps_t[m % 2][:, i * P:(i + 1) * P],
                                                       rows[:, u, TG * k + i, :], ident[:, :])
                        last.then_inc(t_ready[m % 2], 1)
                        if look and k == TGROUPS // 2 - 1:
                            look_up(s + 1, tile_looks(u, 0))
                    if look:
                        look_up(s + 1, tile_looks(u, 1))
                    for i in range(2):
                        pe.wait_ge(t_free[i], turns_done(i, s, u))
                    pe.wait_ge(filled, U * s + u + 1)
                    for v in range(UNITS):
                        for i in range(2):
                            pe.wait_ge(g_free[i], UNITS * (U * s + u) + v + 1)
                        for i in range(UG):
                            b = (v * UG + i) * NG
                            last = nc.tensor.matmul(ps_g[v % 2][:, i, 0:NG * NCOL], xt[:, b:b + NG, :],
                                                    xt[:, b:b + NG, 0:NCOL], start=True, stop=True)
                            if v == 0 and i == 0:
                                last.then_inc(slot_free, 1)
                        last.then_inc(g_ready, 1)
                        if look:
                            look_up(s + 1, tile_looks(u, 2 + v))

                place = 0
                count = [0, 0]

                def layer_place():
                    nonlocal place
                    if look:
                        look_up(s + 1, layer_looks(place))
                    place += 1

                def bank(k):
                    if look or k % 2 == 0:
                        pe.wait_ge(m_free, (N1 + N2 + 1) * s + count[0] + 1)
                        count[0] += 1
                        return ps_m, m_ready
                    pe.wait_ge(l_free, NP * BLOCKS + count[1] + 1)
                    count[1] += 1
                    return ps_l, l_ready

                def results_read():
                    pe.wait_ge(m_free, (N1 + N2 + 1) * s + count[0] + 1)
                    if not look:
                        pe.wait_ge(l_free, NP * BLOCKS + count[1] + 1)

                layer_place()
                pe.wait_ge(f_hi_ready, U * (s + 1))
                for n in range(N1):
                    ps, ready = bank(n)
                    ns = slice(n * P, (n + 1) * P)
                    passes = [(w1x_hi[:, ns], x_hi[:, :]), (w1x_lo[:, ns], x_hi[:, :]), (w1x_hi[:, ns], x_lo[:, :])]
                    for c in range(CH):
                        passes += [(w1_hi[:, c, ns], feat_hi[:, c, :]), (w1_lo[:, c, ns], feat_hi[:, c, :])]
                    first_lo = len(passes)
                    passes += [(w1_hi[:, c, ns], feat_lo[:, c, :]) for c in range(CH)]
                    for i, (w, a) in enumerate(passes):
                        if n == 0 and i == first_lo:
                            pe.wait_ge(f_lo_ready, U * (s + 1))
                        last = nc.tensor.matmul(ps[:, :], w, a, start=(i == 0), stop=(i == len(passes) - 1))
                        if i == len(passes) - 1:
                            last.then_inc(ready, 1)
                        if (i + 1) % (len(passes) // L1_PLACES) == 0:
                            layer_place()
                layer_place()
                results_read()
                for n in range(N2):
                    ps, ready = bank(N1 + n)
                    for k in range(N1):
                        last = nc.tensor.matmul(ps[:, :], w2[:, k, n * P:(n + 1) * P], h1[:, k, :],
                                                start=(k == 0), stop=(k == N1 - 1))
                        if k == N1 - 1:
                            last.then_inc(ready, 1)
                        if k % N2 == N2 - 1:
                            layer_place()
                for _ in range(LAYER_PLACES - place):
                    layer_place()
                results_read()
                ps, ready = bank(N1 + N2)
                for k in range(N2):
                    last = nc.tensor.matmul(ps[0:1, :], w3[:, k:k + 1], h2[:, k, :],
                                            start=(k == 0), stop=(k == N2 - 1))
                last.then_inc(ready, 1)

            look_up(0, range(LOOKS))
            pe.wait_ge(ident_ready, 1)
            pe.wait_ge(pads_ready, 1)
            pe.wait_ge(w1_lo_ready, 2)
            pe.wait_ge(wr_loaded, 16 * (N1 + N2 + N2 + 1))
            with pe.Fori(0, BLOCKS - 1) as s:
                block_steps(s, True)
            block_steps(BLOCKS - 1, False)


_TABLES = 26
_INS = (["r_dense_features", "ids"] + [f"tbl_{f}" for f in range(_TABLES)]
        + ["W_top1", "b_top1", "W_top2", "b_top2", "W_top3"])


def kernel(**inputs):
    import numpy as np
    import concourse.bacc as bacc
    from concourse.bass_utils import run_bass_kernel_spmd

    nc = bacc.Bacc("TRN2", target_bir_lowering=False, num_devices=1)
    given = {name: np.ascontiguousarray(inputs[name]) for name in _INS}
    given["ids_t"] = np.ascontiguousarray(given["ids"].T)
    arrays, ap = {}, {}
    for name, a in given.items():
        arrays[f"in_{name}"] = a
        ap[name] = nc.dram_tensor(f"in_{name}", a.shape, mybir.dt.from_np(a.dtype), kind="ExternalInput").ap()
    out = nc.dram_tensor("out_y", (given["ids"].shape[0], 1), F32, kind="ExternalOutput").ap()
    dlrm_tower(nc, ap["r_dense_features"], ap["ids"], ap["ids_t"], [ap[f"tbl_{f}"] for f in range(_TABLES)],
               ap["W_top1"], ap["b_top1"], ap["W_top2"], ap["b_top2"], ap["W_top3"], out)
    r = run_bass_kernel_spmd(nc, [arrays], core_ids=[0])
    return r.results[0]["out_y"]
```

```python
from contextlib import ExitStack

import concourse.bass as bass
from concourse import mybir

P = 128
Q = 32
F32 = mybir.dt.float32
F32R = mybir.dt.float32r
I32 = mybir.dt.int32
ACT = mybir.ActivationFunctionType
ALU = mybir.AluOpType

PICKED = (2, 3, 17, 18, 19, 21)


def runs(fields):
    out = []
    for at, f in enumerate(fields):
        if out and out[-1][1] + out[-1][2] == f:
            out[-1][2] += 1
        else:
            out.append([at, f, 1])
    return out


def part(n, places, i):
    return range(n * i // places, n * (i + 1) // places)


def dlrm_tower(nc, dense, ids, ids_t, tables, w_top1, b_top1, w_top2, b_top2, w_top3, out):
    B, D = dense.shape
    F = len(tables)
    NF = F + 1
    H1, H2 = w_top1.shape[1], w_top2.shape[1]
    U = 4
    BS = U * P
    BLOCKS = B // BS
    NG = 4
    NCOL = F
    GC = -(-NCOL // 4)
    CH = 4
    UG = 8
    UNITS = P // (NG * UG)
    N1, N2 = H1 // P, H2 // P
    RESULTS = N1 + N2 + 1
    turned = [f for f in range(NF) if f not in PICKED]
    TG = 4
    TGROUPS = -(-len(turned) // TG)
    FIRST_ROWS = TG * (TGROUPS - 2)
    NT = TGROUPS // 2
    NP = len(PICKED)
    V = tables[PICKED[0]].shape[0]
    VC = 8
    VP = V // VC
    RING = 4
    LOOKS = NP * VC
    TILE_LOOKS = 4
    HELD = 2
    LAYER_LOOKS = LOOKS - U * TILE_LOOKS
    EARLY_PLACES = 1 + N1
    LATE_PLACE = EARLY_PLACES + N1 * (CH - 1)
    LAYER_PLACES = LATE_PLACE + 2 * N2 + 1
    assert all(tables[f].shape[0] == V for f in PICKED) and NP % 2 == 0 and V == VC * VP and VP <= P and VC % RING == 0
    assert all(NF - 4 * c - 1 <= 4 * (GC - c) + 1 for c in range(CH, GC))
    assert D == P and NF <= Q and B == BLOCKS * BS and TGROUPS == 6 and U % 2 == 0 and BLOCKS > 1

    with ExitStack() as ctx:
        def sb(name, shape, dt=F32):
            return ctx.enter_context(nc.sbuf_tensor(name, shape, dt))

        def psum(name, shape):
            return ctx.enter_context(nc.psum_tensor(name, shape, F32))

        def sem(name):
            return ctx.enter_context(nc.semaphore(name))

        ident = sb("ident", [P, P])
        ids_now = sb("ids_now", [P, U, F], I32)
        rows = sb("rows", [P, U, len(turned), D])
        xt = sb("xt", [P, P, Q])
        looked = sb("looked", [P, 2, NP, BS])
        raw = sb("raw", [VP, 2, VC, D])
        tbl_hi = sb("tbl_hi", [VP, 2, VC, D], F32R)
        tbl_lo = sb("tbl_lo", [VP, 2, VC, D], F32R)
        ids_row = sb("ids_row", [P, 2, BS], I32)
        onehot = sb("onehot", [VP, RING, BS], F32R)
        row_no = sb("row_no", [P, VC])
        feat = sb("feat", [P, GC, BS])
        feat_hi = sb("feat_hi", [P, CH, BS], F32R)
        feat_lo = sb("feat_lo", [P, CH, BS], F32R)
        x_hi = sb("x_hi", [P, BS], F32R)
        x_lo = sb("x_lo", [P, BS], F32R)
        w1_hi = sb("w1_hi", [P, CH, H1], F32R)
        w1_lo = sb("w1_lo", [P, CH, H1], F32R)
        w1x_hi = sb("w1x_hi", [P, H1], F32R)
        w1x_lo = sb("w1x_lo", [P, H1], F32R)
        w2 = sb("w2", [P, N1, H2])
        w3 = sb("w3", [P, N2])
        b1 = sb("b1", [P, N1])
        b2 = sb("b2", [P, N2])
        h1 = sb("h1", [P, N1, BS])
        h2 = sb("h2", [P, N2, BS])
        y = sb("y", [1, BS])

        late = U - 1
        assert len(turned) * D >= CH * H1 and N1 >= 2
        w1_raw = rows[:, late].rearrange("p f d -> p (f d)")[:, 0:CH * H1].rearrange("p (c n) -> p c n", n=H1)
        w1x_raw = h1

        ps_t = [psum(f"ps_t{i}", [P, TG * P]) for i in range(2)]
        ps_g = [psum(f"ps_g{i}", [P, UG, P]) for i in range(2)]
        ps_l = [psum(f"ps_l{i}", [P, BS]) for i in range(2)]

        ident_zero, ident_ready = sem("ident_zero"), sem("ident_ready")
        row_no_ready = sem("row_no_ready")
        pads_ready = sem("pads_ready")
        w1_zero, w1_loaded, wx_loaded = sem("w1_zero"), sem("w1_loaded"), sem("wx_loaded")
        wx_summed, w1_hi_ready, w1_lo_ready = sem("wx_summed"), sem("w1_hi_ready"), sem("w1_lo_ready")
        wr_loaded = sem("wr_loaded")
        ids_loaded = [sem(f"ids_loaded{u}") for u in range(U)]
        tiles_begun = sem("tiles_begun")
        dense_loaded = [sem(f"dense_loaded{u}") for u in range(U)]
        gathered = [[sem(f"gathered{u}_{i}") for i in range(2)] for u in range(U)]
        slot_free = sem("slot_free")
        raw_loaded = [sem(f"raw_loaded{i}") for i in range(2)]
        hi_ready, lo_ready = sem("hi_ready"), sem("lo_ready")
        onehot_ready = sem("onehot_ready")
        onehot_begun = sem("onehot_begun")
        l_ready, l_free = sem("l_ready"), sem("l_free")
        m_ready, m_free = sem("m_ready"), sem("m_free")
        filled = sem("filled")
        t_ready = [sem(f"t_ready{i}") for i in range(2)]
        t_free = [sem(f"t_free{i}") for i in range(2)]
        g_ready = sem("g_ready")
        g_free = [sem(f"g_free{i}") for i in range(2)]
        moved_early, moved_last = sem("moved_early"), [sem(f"moved_last{c}") for c in range(CH)]
        first_hi_ready, first_lo_ready = sem("first_hi_ready"), sem("first_lo_ready")
        rest_hi_ready, rest_lo_ready = sem("rest_hi_ready"), sem("rest_lo_ready")
        y_stored = sem("y_stored")

        block = ctx.enter_context(nc.Block())

        def pair_row(a, b):
            return D + F + a * (F - 1) - a * (a - 1) // 2 + b - a - 1

        def moved_to(c):
            return c if c < CH else GC - c

        def part_of(early):
            return slice(0, BS - P) if early else slice(BS - P, BS)

        def classes(c):
            return range(min(4, NCOL - 4 * c))

        def moved_from(c):
            return 0 if c < CH else 4 * c + 1

        def before(k):
            return 2 if k >= 2 else k + NP - max(x for x in range(NP) if x % 2 == k % 2)

        def turns_done(s, u, k=TGROUPS):
            return NT * (U * s + u) + k // 2 + 1

        def turn_bank(k):
            return ps_g[0][:, TG * (k % 2):TG * (k % 2) + TG, :].rearrange("p i d -> p (i d)") if k // 2 == 1 \
                else ps_t[k % 2]

        def tile_looks(u, v):
            return [u * TILE_LOOKS + x for x in part(TILE_LOOKS, UNITS, v)]

        def result_bank(k):
            half = UG // 2 * (k % 2)
            return ps_g[k // 2 % 2][:, half:half + UG // 2, :].rearrange("p i b -> p (i b)")

        def layer_looks(i):
            first = 1
            if i == 0:
                return [U * TILE_LOOKS + x for x in range(first)]
            return [U * TILE_LOOKS + first + x for x in part(LAYER_LOOKS - first, LAYER_PLACES - 1, i - 1)]

        def load_ids(eng, s, u):
            eng.dma_start(ids_now[:, u, :], ids[bass.ds(s * BS + u * P, P), :]).then_inc(ids_loaded[u], 16)

        @block.gpsimd
        def _(pool):
            pool.wait_ge(ident_zero, 1)
            nc.gpsimd.affine_select(out=ident[:, :], in_=ident[:, :], compare_op=ALU.not_equal, fill=1.0,
                                    base=0, pattern=[[-1, P]], channel_multiplier=1).then_inc(ident_ready, 1)
            nc.gpsimd.iota(row_no[:, :], pattern=[[1, VC]], base=0, channel_multiplier=VC,
                           allow_small_or_imprecise_dtypes=True).then_inc(row_no_ready, 1)
            with pool.Fori(0, BLOCKS) as s:
                for u in range(U):
                    pool.wait_ge(slot_free, U * s + u + 1)
                    pool.wait_ge(ids_loaded[u], 16 * (s + 1))
                    pool.sem_inc(tiles_begun, 1)
                    for at, f in enumerate(turned[:-1]):
                        pool.indirect_dma_start(
                            rows[:, u, at, :], None, tables[f],
                            bass.IndirectOffsetOnAxis(ids_now[:, u, f:f + 1], 0))\
                            .then_inc(gathered[u][at >= FIRST_ROWS], 16)

        @block.sync
        def _(sp):
            def load_lookup(blk, k, first=False):
                b, f = k % 2, PICKED[k]
                if not (first and k < 2):
                    sp.wait_ge(onehot_ready, VC * (NP * blk + k - before(k) + 1))
                src = tables[f].rearrange("(p c) d -> p c d", c=VC)
                most = VP // 16 * 16
                sp.dma_start(raw[0:most, b], src[0:most]).then_inc(raw_loaded[b], 16)
                sp.dma_start(raw[most:VP, b], src[most:VP]).then_inc(raw_loaded[b], 16)
                sp.dma_start(ids_row[:, b, :], ids_t[f:f + 1, bass.ds(blk * BS, BS)].broadcast_to([P, BS]))\
                    .then_inc(raw_loaded[b], 16)

            def store_y(s):
                sp.wait_ge(m_free, RESULTS * (s + 1) + 1)
                sp.dma_start(out[bass.ds(s * BS, BS), :].rearrange("b o -> o b"), y[:, :]).then_inc(y_stored, 16)

            def move_rows(s, early):
                for i in range(2):
                    sp.wait_ge(g_free[i], UNITS * (U * (s + 1) - early) + 2)
                bs = part_of(early)
                for c in reversed(range(CH, GC)):
                    for j in classes(c):
                        n = NF - moved_from(c)
                        sp.dma_start(feat[Q * j:Q * j + n, moved_to(c), bs],
                                     feat[Q * j + moved_from(c):Q * j + NF, c, bs])\
                            .then_inc(moved_early if early else moved_last[moved_to(c)], 16)

            load_ids(sp, 0, 0)
            for k in range(2):
                load_lookup(0, k, first=True)
            sp.dma_start(w1x_raw[:, 0, :], w_top1[0:D, :]).then_inc(wx_loaded, 16)
            sp.dma_start(w1x_raw[:, 1, :], w_top1[w_top1.shape[0] - D:, :]).then_inc(wx_loaded, 16)
            sp.wait_ge(w1_zero, 1)
            for a in range(F - 1):
                if a in (F // 2, 3 * F // 4):
                    load_lookup(0, 2 + (a > F // 2), first=True)
                c, j = a // 4, a % 4
                up = Q * j - moved_from(c)
                sp.dma_start(w1_raw[up + a + 1:up + F, moved_to(c), :],
                             w_top1[pair_row(a, a + 1):pair_row(a, F - 1) + 1, :]).then_inc(w1_loaded, 16)
            for j in range(4):
                sp.dma_start(w1_raw[Q * j + F:Q * j + F + 1, :, :],
                             w_top1[D + j:D + 4 * CH:4, :].unsqueeze(0)).then_inc(w1_loaded, 16)
            load_lookup(0, 4, first=True)
            for a in range(4 * CH, F):
                c, j = a // 4, a % 4
                at = Q * j + F - moved_from(c)
                sp.dma_start(w1_raw[at:at + 1, moved_to(c), :], w_top1[D + a:D + a + 1, :]).then_inc(w1_loaded, 16)
            for k in range(5, NP):
                load_lookup(0, k, first=True)
            with sp.Fori(0, BLOCKS - 1) as s:
                for k in range(3):
                    load_lookup(s + 1, k)
                move_rows(s, 1)
                load_lookup(s + 1, 3)
                move_rows(s, 0)
                for k in range(4, NP):
                    load_lookup(s + 1, k)
                store_y(s)
            for early in (1, 0):
                move_rows(BLOCKS - 1, early)
            store_y(BLOCKS - 1)
            sp.wait_ge(y_stored, 16 * (BLOCKS + 1))

        def move_transposed(eng, copy, s, u, k):
            eng.wait_ge(t_ready[k % 2], NT * (U * s + u) + k // 2 + 1)
            for at, f, n in runs(turned[TG * k:TG * k + TG]):
                last = copy(xt[:, :, f:f + n],
                            turn_bank(k)[:, at * P:(at + n) * P].rearrange("p (f b) -> p b f", f=n))
            last.then_inc(t_free[k % 2], 1)

        def move_gram(eng, copy, mine, quads, s, u, v):
            eng.wait_ge(g_ready, UNITS * (U * s + u) + v + 1)
            for q in quads:
                for j in range(4):
                    src = ps_g[v % 2][Q * q:Q * q + Q, :, q * NCOL + j:(q + 1) * NCOL:4]
                    b = u * P + v * NG * UG + q
                    dst = feat[Q * j:Q * j + Q, 0:len(range(j, NCOL, 4)), b:b + NG * (UG - 1) + 1:NG].rearrange("p c i -> p i c")
                    last = copy(dst, src)
            last.then_inc(g_free[mine], 1)

        @block.vector
        def _(dve):
            def move_looked(blk, k):
                dve.wait_ge(l_ready, NP * blk + k + 1)
                nc.vector.tensor_copy(looked[:, blk % 2, k, :], ps_l[k % 2][:, :]).then_inc(l_free, 1)

            def make_onehots(blk, chunks):
                for x in chunks:
                    k, c = divmod(x, VC)
                    b = k % 2
                    if c == 0:
                        dve.wait_ge(hi_ready, NP * blk + k + 1)
                        nc.vector.tensor_tensor(tbl_lo[:, b], raw[:, b], tbl_hi[:, b].bitcast(F32),
                                                ALU.subtract).then_inc(lo_ready, 1)
                    dve.wait_ge(onehot_begun, LOOKS * blk + x + 1)
                    nc.vector.tensor_tensor(onehot[:, c % RING, :], ids_row[0:VP, b, :],
                                            row_no[0:VP, c:c + 1].broadcast_to([VP, BS]),
                                            ALU.is_equal).then_inc(onehot_ready, 1)
                    if c == RING - 2 and k > 0:
                        move_looked(blk, k - 1)

            def block_steps(s, look):
                def split_first(u):
                    bs = slice(u * P, (u + 1) * P)
                    dve.wait_ge(first_hi_ready, U * s + u + 1)
                    nc.vector.tensor_tensor(feat_lo[:, 0, bs], feat[:, 0, bs], feat_hi[:, 0, bs].bitcast(F32),
                                            ALU.subtract).then_inc(first_lo_ready, 1)

                def split_rest(early, c, end):
                    bs = part_of(early)
                    dve.wait_ge(rest_hi_ready, CH * s + 1 + (0 if early else c))
                    nc.vector.tensor_tensor(feat_lo[:, c:end, bs], feat[:, c:end, bs],
                                            feat_hi[:, c:end, bs].bitcast(F32), ALU.subtract)\
                        .then_inc(rest_lo_ready, 1)

                for u in range(U):
                    for k in range(0, TGROUPS, 2):
                        move_transposed(dve, nc.vector.tensor_copy, s, u, k)
                    dve.wait_ge(t_free[1], turns_done(s, u))
                    bs = slice(u * P, (u + 1) * P)
                    nc.vector.tensor_tensor(x_lo[:, bs], xt[:, :, F], x_hi[:, bs].bitcast(F32), ALU.subtract)
                    for v in range(UNITS):
                        if look:
                            make_onehots(s + 1, tile_looks(u, v))
                        if u > 0 and v == 0:
                            split_first(u - 1)
                        move_gram(dve, nc.vector.tensor_copy, 0, (0, 1), s, u, v)
                split_first(U - 1)
                for i in range(3):
                    if look:
                        make_onehots(s + 1, layer_looks(i))
                split_rest(1, 1, CH)
                for i in range(3, EARLY_PLACES):
                    if look:
                        make_onehots(s + 1, layer_looks(i))
                for c in range(1, CH):
                    split_rest(0, c, c + 1)
                    for i in range(N1):
                        if look:
                            make_onehots(s + 1, layer_looks(EARLY_PLACES + N1 * (c - 1) + i))
                if look:
                    for i in range(LATE_PLACE, LAYER_PLACES):
                        make_onehots(s + 1, layer_looks(i))
                    move_looked(s + 1, NP - 1)

            nc.vector.memset(ident[:, :], 0.0).then_inc(ident_zero, 1)
            dve.sem_inc(slot_free, late)
            dve.sem_inc(t_free[0], 1)
            dve.sem_inc(g_free[0], 2)
            dve.sem_inc(l_free, 2)
            dve.sem_inc(onehot_begun, RING - 1)
            nc.vector.memset(w1_raw[:, :, :], 0.0).then_inc(w1_zero, 1)
            nc.vector.memset(xt[:, :, NF:Q], 0.0).then_inc(pads_ready, 1)
            dve.wait_ge(row_no_ready, 1)
            make_onehots(0, range(LOOKS))
            dve.wait_ge(wx_loaded, 32)
            nc.vector.tensor_tensor(w1x_raw[:, 0, :], w1x_raw[:, 0, :], w1x_raw[:, 1, :], ALU.add)\
                .then_inc(wx_summed, 1)
            dve.wait_ge(w1_hi_ready, 2)
            nc.vector.tensor_tensor(w1_lo[:, :, :], w1_raw[:, :, :], w1_hi[:, :, :].bitcast(F32),
                                    ALU.subtract).then_inc(w1_lo_ready, 1)
            nc.vector.tensor_tensor(w1x_lo[:, :], w1x_raw[:, 0, :], w1x_hi[:, :].bitcast(F32), ALU.subtract)\
                .then_inc(w1_lo_ready, 1)
            move_looked(0, NP - 1)
            dve.wait_ge(w1_lo_ready, 2)
            dve.sem_inc(slot_free, U - late)
            dve.wait_ge(wr_loaded, 16 * (N1 + N2 + N2 + 1))
            with dve.Fori(0, BLOCKS - 1) as s:
                block_steps(s, True)
            block_steps(BLOCKS - 1, False)

        @block.scalar
        def _(act):
            def split_table(blk, k, first=False):
                b = k % 2
                act.wait_ge(raw_loaded[b], 48 * (len(range(b, NP, 2)) * blk + k // 2 + 1))
                if not (first and k < 2):
                    act.wait_ge(l_ready, NP * blk + k - before(k) + 1)
                nc.scalar.copy(tbl_hi[:, b], raw[:, b]).then_inc(hi_ready, 1)

            def split_tables(blk, chunks, first=False):
                for x in chunks:
                    if x % VC == VC // 2 and x // VC + 1 < NP:
                        split_table(blk, x // VC + 1, first)

            def load_dense(s, u):
                act.dma_start(rows[:, u, len(turned) - 1, :], dense[bass.ds(s * BS + u * P, P), :])\
                    .then_inc(dense_loaded[u], 16)

            def block_steps(s, look):
                def split_first(u):
                    for i in range(2):
                        act.wait_ge(g_free[i], UNITS * (U * s + u + 1) + 2)
                    bs = slice(u * P, (u + 1) * P)
                    nc.scalar.copy(feat_hi[:, 0, bs], feat[:, 0, bs]).then_inc(first_hi_ready, 1)

                def split_rest(early, c, end):
                    bs = part_of(early)
                    if early:
                        act.wait_ge(moved_early, 16 * sum(len(classes(g)) for g in range(CH, GC)) * (s + 1))
                    else:
                        act.wait_ge(moved_last[c], 16 * len(classes(GC - c)) * (s + 1))
                    nc.scalar.copy(feat_hi[:, c:end, bs], feat[:, c:end, bs]).then_inc(rest_hi_ready, 1)

                for u in range(U):
                    bs = slice(u * P, (u + 1) * P)
                    act.wait_ge(l_free, NP * (s + 1) + 2)
                    for at, f, n in runs(PICKED):
                        last = nc.scalar.copy(xt[:, :, f:f + n],
                                              looked[:, s % 2, at:at + n, bs].rearrange("p f b -> p b f"))
                    last.then_inc(filled, 1)
                    for k in (1, 3):
                        move_transposed(act, nc.scalar.copy, s, u, k)
                    k = TGROUPS - 1
                    at = len(turned) - 1 - TG * k
                    act.wait_ge(t_ready[k % 2], NT * (U * s + u) + k // 2 + 1)
                    nc.scalar.copy(x_hi[:, bs], turn_bank(k)[:, at * P:(at + 1) * P])
                    move_transposed(act, nc.scalar.copy, s, u, k)
                    if u > 0:
                        split_first(u - 1)
                    elif look:
                        split_table(s + 1, 0)
                    for v in range(UNITS):
                        if look:
                            split_tables(s + 1, tile_looks(u, v))
                        move_gram(act, nc.scalar.copy, 1, (2, 3), s, u, v)
                        if look and v == 1:
                            load_ids(act, s + 1, u)
                            load_dense(s + 1, u)
                split_first(U - 1)
                split_rest(1, 1, CH)
                if look:
                    for i in range(EARLY_PLACES):
                        split_tables(s + 1, layer_looks(i))
                for c in range(1, CH):
                    split_rest(0, c, c + 1)
                    for i in range(N1):
                        if look:
                            split_tables(s + 1, layer_looks(EARLY_PLACES + N1 * (c - 1) + i))
                outs = [(h1[:, n], b1[:, n:n + 1]) for n in range(N1)] + [(h2[:, n], b2[:, n:n + 1])
                                                                        for n in range(N2)]
                for k, (dst, bias) in enumerate(outs):
                    if look and k >= N1:
                        for i in range(2):
                            split_tables(s + 1, layer_looks(LATE_PLACE + 2 * (k - N1) + i))
                    act.wait_ge(m_ready, RESULTS * s + k + 1)
                    nc.scalar.activation(dst, result_bank(k), ACT.Relu, bias=bias).then_inc(m_free, 1)
                if look:
                    split_tables(s + 1, layer_looks(LAYER_PLACES - 1))
                act.wait_ge(m_ready, RESULTS * (s + 1))
                act.wait_ge(y_stored, 16 * (s + 1))
                nc.scalar.copy(y[:, :], result_bank(RESULTS - 1)[0:1, :]).then_inc(m_free, 1)

            act.sem_inc(t_free[1], 1)
            act.sem_inc(g_free[1], 2)
            act.sem_inc(m_free, 1)
            act.sem_inc(y_stored, 16)
            for u in range(1, U):
                load_ids(act, 0, u)
            for u in range(late):
                load_dense(0, u)
            split_table(0, 0, first=True)
            split_table(0, 1, first=True)
            act.dma_start(w2[:, :, :], w_top2.rearrange("(k p) n -> p k n", p=P)).then_inc(wr_loaded, 16)
            for k in range(N2):
                act.dma_start(w3[:, k:k + 1], w_top3[k * P:(k + 1) * P, :]).then_inc(wr_loaded, 16)
            for k in range(N1):
                act.dma_start(b1[:, k:k + 1], b_top1[k * P:(k + 1) * P].unsqueeze(1)).then_inc(wr_loaded, 16)
            for k in range(N2):
                act.dma_start(b2[:, k:k + 1], b_top2[k * P:(k + 1) * P].unsqueeze(1)).then_inc(wr_loaded, 16)
            split_tables(0, range(VC, LOOKS), first=True)
            act.wait_ge(w1_loaded, 16 * (F - 1 + 4 + F - 4 * CH))
            nc.scalar.copy(w1_hi[:, :, :], w1_raw[:, :, :]).then_inc(w1_hi_ready, 1)
            act.wait_ge(wx_summed, 1)
            nc.scalar.copy(w1x_hi[:, :], w1x_raw[:, 0, :]).then_inc(w1_hi_ready, 1)
            act.wait_ge(w1_lo_ready, 2)
            for u in range(late, U):
                load_dense(0, u)
            act.wait_ge(wr_loaded, 16 * (N1 + N2 + N2 + 1))
            with act.Fori(0, BLOCKS - 1) as s:
                block_steps(s, True)
            block_steps(BLOCKS - 1, False)

        @block.tensor
        def _(pe):
            def look_up(blk, chunks):
                for x in chunks:
                    k, c = divmod(x, VC)
                    b = k % 2
                    if c == 0:
                        pe.wait_ge(l_free, NP * blk + k + 1)
                        pe.wait_ge(lo_ready, NP * blk + k + 1)
                    pe.wait_ge(onehot_ready, LOOKS * blk + x + 1)
                    nc.tensor.matmul(ps_l[b][:, :], tbl_hi[:, b, c, :], onehot[:, c % RING, :],
                                     start=(c == 0), stop=False).then_inc(onehot_begun, 1)
                    last = nc.tensor.matmul(ps_l[b][:, :], tbl_lo[:, b, c, :], onehot[:, c % RING, :],
                                            start=False, stop=(c == VC - 1))
                    if c == VC - 1:
                        last.then_inc(l_ready, 1)

            def block_steps(s, look):
                looks_done = 0

                def look_up_to(x):
                    nonlocal looks_done
                    look_up(s + 1, range(looks_done, x))
                    looks_done = max(looks_done, x)

                for u in range(U):
                    pe.wait_ge(gathered[u][0], 16 * FIRST_ROWS * (s + 1))
                    for k in range(TGROUPS):
                        if k == TGROUPS - 2:
                            pe.wait_ge(gathered[u][1], 16 * (len(turned) - 1 - FIRST_ROWS) * (s + 1))
                            pe.wait_ge(dense_loaded[u], 16 * (s + 1))
                        if k == 2:
                            for i in range(2):
                                pe.wait_ge(g_free[i], UNITS * (U * s + u) + 1)
                            if u == 0:
                                pe.wait_ge(m_free, RESULTS * s + 1)
                        elif k // 2 != 1:
                            pe.wait_ge(t_free[k % 2], turns_done(s, u, max(k - 2, 0)))
                        for i in range(min(TG, len(turned) - TG * k)):
                            last = nc.tensor.transpose(turn_bank(k)[:, i * P:(i + 1) * P],
                                                       rows[:, u, TG * k + i, :], ident[:, :])
                        last.then_inc(t_ready[k % 2], 1)
                    if look:
                        look_up_to(u * TILE_LOOKS)
                    for i in range(2):
                        pe.wait_ge(t_free[i], turns_done(s, u))
                    pe.wait_ge(filled, U * s + u + 1)
                    for v in range(UNITS):
                        for i in range(2):
                            pe.wait_ge(g_free[i], UNITS * (U * s + u) + v + 1)
                        for i in range(UG):
                            b = (v * UG + i) * NG
                            last = nc.tensor.matmul(ps_g[v % 2][:, i, 0:NG * NCOL], xt[:, b:b + NG, :],
                                                    xt[:, b:b + NG, 0:NCOL], start=True, stop=True)
                            if v == 0 and i == 0:
                                last.then_inc(slot_free, 1)
                        last.then_inc(g_ready, 1)
                        if look:
                            look_up_to(u * TILE_LOOKS + (TILE_LOOKS - HELD) * (v + 1) // UNITS)

                place = 0

                def layer_place():
                    nonlocal place
                    if look:
                        look_up_to(max([looks_done] + [x + 1 for x in layer_looks(place)]))
                    place += 1

                def results_read(n):
                    pe.wait_ge(m_free, RESULTS * s + n + 1)

                def layer1(n, passes, first, last):
                    for i, (w, a) in enumerate(passes):
                        mm = nc.tensor.matmul(result_bank(n), w[..., n * P:(n + 1) * P], a,
                                              start=(first and i == 0), stop=(last and i == len(passes) - 1))
                    return mm

                for n in range(N1):
                    if n % 2 == 0:
                        for i in range(2):
                            pe.wait_ge(g_free[i], UNITS * U * (s + 1) + 1 + n // 2)
                    layer1(n, [(w1x_hi, x_hi[:, :]), (w1x_lo, x_hi[:, :]), (w1x_hi, x_lo[:, :])], True, False)
                layer_place()
                for n in range(N1):
                    if n == 0:
                        pe.wait_ge(first_hi_ready, U * (s + 1))
                        pe.wait_ge(first_lo_ready, U * (s + 1))
                    layer1(n, [(w1_hi[:, 0], feat_hi[:, 0, :]), (w1_lo[:, 0], feat_hi[:, 0, :]),
                               (w1_hi[:, 0], feat_lo[:, 0, :])], False, False)
                    layer_place()
                for c in range(1, CH):
                    pe.wait_ge(rest_hi_ready, CH * s + c + 1)
                    pe.wait_ge(rest_lo_ready, CH * s + c + 1)
                    for n in range(N1):
                        mm = layer1(n, [(w1_hi[:, c], feat_hi[:, c, :]), (w1_lo[:, c], feat_hi[:, c, :]),
                                        (w1_hi[:, c], feat_lo[:, c, :])], False, c == CH - 1)
                        if c == CH - 1:
                            mm.then_inc(m_ready, 1)
                        layer_place()
                for n in range(N2):
                    for k in range(N1):
                        if n == 0:
                            results_read(k + 1)
                        last = nc.tensor.matmul(result_bank(N1 + n), w2[:, k, n * P:(n + 1) * P], h1[:, k, :],
                                                start=(k == 0), stop=(k == N1 - 1))
                        if k == N1 - 1:
                            last.then_inc(m_ready, 1)
                        if k % 2 == 1:
                            layer_place()
                for k in range(N2):
                    results_read(N1 + k + 1)
                    last = nc.tensor.matmul(result_bank(RESULTS - 1)[0:1, :], w3[:, k:k + 1], h2[:, k, :],
                                            start=(k == 0), stop=(k == N2 - 1))
                last.then_inc(m_ready, 1)
                layer_place()
                assert place == LAYER_PLACES

            look_up(0, range(LOOKS))
            pe.wait_ge(ident_ready, 1)
            pe.wait_ge(pads_ready, 1)
            pe.wait_ge(w1_lo_ready, 2)
            pe.wait_ge(wr_loaded, 16 * (N1 + N2 + N2 + 1))
            with pe.Fori(0, BLOCKS - 1) as s:
                block_steps(s, True)
            block_steps(BLOCKS - 1, False)


_TABLES = 26
_INS = (["r_dense_features", "ids"] + [f"tbl_{f}" for f in range(_TABLES)]
        + ["W_top1", "b_top1", "W_top2", "b_top2", "W_top3"])


def kernel(**inputs):
    import numpy as np
    import concourse.bacc as bacc
    from concourse.bass_utils import run_bass_kernel_spmd

    nc = bacc.Bacc("TRN2", target_bir_lowering=False, num_devices=1)
    given = {name: np.ascontiguousarray(inputs[name]) for name in _INS}
    given["ids_t"] = np.ascontiguousarray(given["ids"].T)
    arrays, ap = {}, {}
    for name, a in given.items():
        arrays[f"in_{name}"] = a
        ap[name] = nc.dram_tensor(f"in_{name}", a.shape, mybir.dt.from_np(a.dtype), kind="ExternalInput").ap()
    out = nc.dram_tensor("out_y", (given["ids"].shape[0], 1), F32, kind="ExternalOutput").ap()
    dlrm_tower(nc, ap["r_dense_features"], ap["ids"], ap["ids_t"], [ap[f"tbl_{f}"] for f in range(_TABLES)],
               ap["W_top1"], ap["b_top1"], ap["W_top2"], ap["b_top2"], ap["W_top3"], out)
    r = run_bass_kernel_spmd(nc, [arrays], core_ids=[0])
    return r.results[0]["out_y"]
```
